# Optimizing a Trainium2 kernel written in Bass

```python
import numpy as np
import jax
import jax.numpy as jnp

def _softmax(x, axis=-1):
    return jax.nn.softmax(x, axis=axis)

def _gelu(x):
    return jax.nn.gelu(x, approximate=True)

def _silu(x):
    return jax.nn.silu(x)

def _sigmoid(x):
    return jax.nn.sigmoid(x)

def _layernorm(x, axis=-1, eps=1e-05):
    m = jnp.mean(x, axis=axis, keepdims=True)
    v = jnp.var(x, axis=axis, keepdims=True)
    return (x - m) / jnp.sqrt(v + eps)

def _scatter_add(tgt, idx, src, axis=0):
    return tgt.at[idx].add(src)

def _segment_sum(src, seg, n):
    return jax.ops.segment_sum(src, seg, n)
kernel_name = 'mk_gnn_preln_d1_gnn_r8_358d78'

def setup_inputs(seed: int=0):
    np.random.seed(seed)
    _w = jnp.asarray

    def _rec_inputs():
        import jax
        import jax.numpy as jnp
        _gk = jax.random.key(seed)
        x = -4.129e-05 + 1 * jax.random.normal(jax.random.fold_in(_gk, 1), (6250, 128), jnp.float32)
        src = jax.random.randint(jax.random.fold_in(_gk, 2), (200000,), 0, 6250, jnp.int32)
        dst = jax.random.randint(jax.random.fold_in(_gk, 3), (200000,), 0, 6250, jnp.int32)
        _o = jnp.argsort(dst, stable=True)
        src = src[_o]
        dst = dst[_o]
        edge_type_16 = jax.random.randint(jax.random.fold_in(_gk, 12), (200000,), 0, 16, jnp.int32)
        return (x, src, dst, edge_type_16)
    x, src, dst, edge_type_16 = _rec_inputs()

    def _L0_gnn_setup():
        import jax, jax.numpy as jnp
        import numpy as np
        N_NODES = 6250
        N_REL = 16
        EMB = 128
        N_BASES = 16
        N_EDGES = 125000
        key = jax.random.key(seed)
        ks = jax.random.split(key, 9)
        src = jax.random.randint(ks[0], (N_EDGES,), 0, N_NODES)
        rel = jax.random.randint(ks[1], (N_EDGES,), 0, N_REL)
        dst = jax.random.randint(ks[2], (N_EDGES,), 0, N_NODES)
        embeddings = jax.random.normal(ks[3], (N_NODES, EMB), dtype=jnp.float32)
        tokeys = jax.random.normal(ks[4], (EMB, EMB), dtype=jnp.float32) / np.sqrt(EMB)
        toqueries = jax.random.normal(ks[5], (EMB, EMB), dtype=jnp.float32) / np.sqrt(EMB)
        relations = jax.random.normal(ks[6], (N_REL, EMB), dtype=jnp.float32)
        comps = jax.random.normal(ks[7], (N_REL, N_BASES), dtype=jnp.float32) / np.sqrt(N_BASES)
        bases_w = jax.random.normal(ks[8], (N_BASES, EMB, EMB), dtype=jnp.float32) / np.sqrt(EMB)
        return {'src': src, 'rel': rel, 'dst': dst, 'embeddings': embeddings, 'tokeys': tokeys, 'toqueries': toqueries, 'relations': relations, 'comps': comps, 'bases_w': bases_w}
    _L0_gnn_all = _L0_gnn_setup()
    _L0_gnn_in = {k: v for k, v in _L0_gnn_all.items() if k in ('tokeys', 'toqueries', 'relations', 'comps', 'bases_w')}
    del _L0_gnn_all
    return {'x': x, 'src': src, 'dst': dst, 'edge_type_16': edge_type_16, 'L0_gnn_tokeys': _L0_gnn_in['tokeys'], 'L0_gnn_toqueries': _L0_gnn_in['toqueries'], 'L0_gnn_relations': _L0_gnn_in['relations'], 'L0_gnn_comps': _L0_gnn_in['comps'], 'L0_gnn_bases_w': _L0_gnn_in['bases_w']}

def reference(x, src, dst, edge_type_16, L0_gnn_tokeys, L0_gnn_toqueries, L0_gnn_relations, L0_gnn_comps, L0_gnn_bases_w):
    import jax
    import jax.numpy as jnp

    def _L0_gnn_ref(src, rel, dst, embeddings, tokeys, toqueries, relations, comps, bases_w):
        import jax, jax.numpy as jnp
        import numpy as np
        N_NODES = 6250
        N_REL = 16
        EMB = 128
        N_BASES = 16
        N_EDGES = 125000
        n, e = embeddings.shape
        r = relations.shape[0]
        si, pi, oi = (src, rel, src)
        semb = embeddings[si] @ tokeys.T
        oemb = embeddings[oi] @ toqueries.T
        pemb = relations[pi]
        dots = jnp.sum(semb * pemb * oemb, axis=1) / e
        values = jnp.exp(dots)
        fr = src + n * rel
        to = dst
        rowsum = jax.ops.segment_sum(values, fr, num_segments=r * n)
        values = values / rowsum[fr]
        msgs = values[:, None] * embeddings[to]
        output = jax.ops.segment_sum(msgs, fr, num_segments=r * n)
        output = output.reshape(r, n, e)
        weights = jnp.einsum('rb,bij->rij', comps, bases_w)
        out = jnp.einsum('rij,rnj->ni', weights, output)
        return jax.nn.relu(out)
    h = jnp.maximum(_layernorm(x, axis=-1), 0.0)
    x = x + _L0_gnn_ref(src, edge_type_16, dst, h, L0_gnn_tokeys, L0_gnn_toqueries, L0_gnn_relations, L0_gnn_comps, L0_gnn_bases_w)
    return x

_drawn_inputs = setup_inputs


def setup_inputs(seed=0):
    import zlib

    import numpy as np

    out = dict(_drawn_inputs(seed))
    spreads = {}
    factors = {}
    for name, (base, spread) in spreads.items():
        noise = np.random.default_rng([zlib.crc32(name.encode()), seed]).standard_normal(out[name].shape)
        drawn = base * np.exp(spread * noise) if base else spread * noise
        out[name] = jnp.asarray(drawn.astype(out[name].dtype))
    for name, factor in factors.items():
        out[name] = (out[name] * factor).astype(out[name].dtype)
    return out
```

```python
from contextlib import ExitStack

import concourse.bass as bass
from concourse import mybir
from concourse.alu_op_type import AluOpType as ALU

ACT = mybir.ActivationFunctionType
AX = mybir.AxisListType
F32 = mybir.dt.float32
F16 = mybir.dt.float16
BF16 = mybir.dt.bfloat16
I32 = mybir.dt.int32

P = 128
EMB = 128
EPS = 1e-5


def program(nc, x, src, dst, rel, tokeys, toqueries, relations, comps, bases_w, out):
    N = x.shape[0]
    E = src.shape[0]
    R = relations.shape[0]
    NBASE = comps.shape[1]
    assert R == 16 and NBASE == 16 and x.shape[1] == EMB

    NB = -(-N // P)
    LASTN = N - (NB - 1) * P
    EP = 125
    NCOL = E // EP
    TC = 32
    NCH = NCOL // TC
    assert E == EP * NCOL and NCOL == NCH * TC
    WIN = 128
    G = 36
    BCAP = G * P
    STRIDE = 2 * BCAP
    NREC = NB * STRIDE
    BIG = 2048.0
    SENT = N << 11
    ZROWS = N * R + 1

    Z = nc.dram_tensor("Z_messages", (ZROWS, EMB), F32, kind="Internal").ap()
    stream = nc.dram_tensor("bucket_streams", (NREC // P, P), F32, kind="Internal").ap()

    with ExitStack() as ctx:
        def sb(name, shape, dt):
            return ctx.enter_context(nc.sbuf_tensor(name, shape, dt))

        def sem(name):
            return ctx.enter_context(nc.semaphore(name))

        bank = [ctx.enter_context(nc.psum_tensor(f"bank{i}", [P, 512], F32)) for i in range(8)]

        arena = sb("arena", [P, 3 * G * EMB], F32)
        Q = P // NBASE
        bases = arena[:, 0:EMB * EMB // Q].rearrange("p (h j) -> p h j", j=EMB)
        Gbuf = [arena[:, p * G * EMB:(p + 1) * G * EMB].rearrange("p (k i) -> p k i", k=G) for p in range(2)]
        OW = arena[:, 2 * G * EMB:3 * G * EMB].rearrange("p (k n) -> p k n", k=G)
        marks = arena[0:NB, 2 * G * EMB:3 * G * EMB]

        stage = sb("stage", [P, 8192], F32)
        raw = [stage[0:EP, k * NCOL:(k + 1) * NCOL].bitcast(I32) for k in range(5)]
        ZS = [stage[:, p * 2048:(p + 1) * 2048] for p in range(2)]
        OHS = [stage[0:EP, 4096 + p * 2048:4096 + (p + 1) * 2048].bitcast(F16)
               .rearrange("p (s t) -> p s t", s=WIN) for p in range(2)]
        OHN = [stage[:, p * G * 64:(p + 1) * G * 64].bitcast(BF16).rearrange("p (k n) -> p k n", k=G) for p in range(2)]

        HALF = NB * R // 2
        GCH = -(-NB * EMB // 512)
        gen_nloc = stage[0:EP, 0:NCOL]
        gen_rel = stage[0:EP, NCOL:2 * NCOL]
        gen_cnt = stage[:, 4 * NCOL:4 * NCOL + NB * R]
        gen_cnt_half = [gen_cnt[:, k * HALF:(k + 1) * HALF] for k in range(2)]
        gen_w = stage[:, 4 * NCOL + NB * R:4 * NCOL + 2 * NB * R]
        gen_acc = arena[:, 0:NB * EMB]
        gen_msg_flat = arena[0:EP, NB * EMB:2 * NB * EMB]
        gen_msg = gen_msg_flat.rearrange("p (b i) -> p b i", i=EMB)
        gen_picked = gen_msg_flat[:, 0:NB * R]
        gen_br_flat = arena[0:EP, 2 * NB * EMB:2 * NB * EMB + NB * R]
        gen_br = gen_br_flat.rearrange("p (b r) -> p b r", r=R)

        X = sb("X", [P, NB, EMB], F32)
        stats = sb("stats", [P, NB, 6], F32)
        mv = sb("mean_var", [P, NB, 2], F32)
        rstd = sb("rstd", [P, NB], F32)
        std = sb("std", [P, NB], F32)
        epsc = sb("eps_col", [P, 1], F32)

        q16 = sb("q16", [EP, NCOL], F16)
        hi16 = sb("hi16", [EP, NCOL], F16)
        lo16 = sb("lo16", [EP, NCOL], F16)
        iotaB = sb("iotaB", [EP, NB, TC], F16)
        iotaS = sb("iotaS", [EP, WIN, TC], F16)
        restart = sb("restart", [EP, NB, TC], F16)
        iotaN = sb("iotaN", [P, P], BF16)
        identf = sb("identf", [P, P], F32)
        ident4k = sb("ident4k", [P, P], F32)
        ident16 = sb("ident16", [P, P], F16)
        identb = sb("identb", [P, P], BF16)
        before16 = sb("before16", [EP, EP], F16)
        ones16 = sb("ones16", [EP, 1], F16)

        OHB = [sb(f"OHB{p}", [EP, NB, TC], F16) for p in range(2)]
        SC = [sb(f"SC{p}", [EP, NB, TC], F16) for p in range(2)]
        PFS = sb("PFS", [EP, NB, TC], F16)
        M = sb("M", [EP, NB, TC], F16)
        COUNT = [sb(f"COUNT{p}", [NB, 1], F32) for p in range(2)]
        RK16 = sb("RK16", [EP, TC], F16)
        pay_all = sb("pay_all", [P, 2, TC * 2 * NB], F16)
        PAY = [pay_all[0:EP, p, :].rearrange("p (x b t) -> p x b t", t=TC, x=2) for p in range(2)]
        OHT = pay_all[:, :, :].rearrange("p a b -> p (a b)")[:, 0:G * P].bitcast(BF16)\
            .rearrange("p (k e) -> p k e", k=G)
        DS = [sb(f"DS{p}", [P, 2 * NB], F32) for p in range(2)]
        REC = [sb(f"REC{p}", [NB, WIN], F32) for p in range(2)]
        POS = sb("POS", [NB, NCH + 1], F32)
        LIM = sb("LIM", [NB, 1], F32)
        POSI = sb("POSI", [NB, 1], I32)
        MX = sb("MX", [NB, 1], F32)
        IDXW = [sb(f"IDXW{p}", [NB, 1], I32) for p in range(2)]

        wload = sb("wload", [P, 2, EMB], F32)
        rload = sb("rload", [R, EMB + NBASE], F32)
        KQT = sb("KQT", [P, 2, EMB], F32)
        relT = sb("relT", [P, R], F32)
        compsT = sb("compsT", [NBASE, R], F32)
        spread = sb("spread", [NBASE, NBASE, P // NBASE], F32)
        QI = sb("QI", [P, 2], I32)
        qmask = sb("qmask", [P, P // NBASE], F32)
        compsB = sb("compsB", [P, R], F32)
        compsD = sb("compsD", [P, P // NBASE, R], F32)
        WT = sb("WT", [P, R, EMB], F32)
        H = sb("H", [P, EMB], F32)
        HT = [sb(f"HT{p}", [P, P], F32) for p in range(2)]
        SO = sb("SO", [P, 2 * P], F32)
        PR = [sb(f"PR{p}", [P, P], F32) for p in range(2)]
        V = sb("V", [P, NB, R], F32)
        zrow = sb("zrow", [1, EMB], F32)

        NT = sb("NT", [NB, 6], F32)
        NTI = sb("NTI", [NB, 2], I32)
        ROWI = sb("ROWI", [1, 3 * NB + 1], I32)
        upto16 = sb("upto16", [NB, NB], F32)
        PARI = sb("PARI", [NB, 2], I32)
        RL = [sb(f"RL{p}", [G, P], F32) for p in range(2)]
        RI = sb("RI", [P, G], I32)
        IDX = [sb(f"IDX{p}", [P, G], I32) for p in range(2)]
        NLI = sb("NLI", [P, 2, G], I32)
        NLF = sb("NLF", [P, G], BF16)
        INV = sb("INV", [P, G], F32)
        RRF = sb("RRF", [P, G], BF16)
        OHR = [sb(f"OHR{p}", [P, G, R], BF16) for p in range(2)]
        WC = sb("WC", [P, 6, R], F32)
        W3 = sb("W3", [P, 3, R], BF16)
        M2 = sb("M2", [P, 9, 3, R], F32)
        WE = [sb(f"WE{p}", [P, G], F32) for p in range(2)]
        O = [sb(f"O{p}", [P, EMB], F32) for p in range(2)]

        small = M2[0:EP, 0:4, :, :].rearrange("p k x r -> p (k x r)")
        gen_bucket, gen_bw = small[:, 0:NB], small[:, 64:64 + NB]
        gen_r, gen_we = small[:, 128:128 + R], small[:, 160:161]
        gen_node = PR[0][0:EP, :]
        gen_nodeT = HT[0][:, 0:EP]
        gen_rows = SO[0:EP, 0:EMB]
        gen_idx = RI[0:EP, 0:1]

        names = """const x_in w_in bases_in edges_in kq_t kq_sb wt_mm wt_sb comps_d edge edges_done
            stat varr stdd ln ohb scan pf pfread ncount own m_sum ohs idxw mx pos pay d_mm d_sb rec_mm rec_sb scat
            h th ht so_mm so_sb prod z_mm z_sb zst0 zst1 zrow v nt nt_mm nt_row marks_sb marks_st
            rl0 rl1 rl_t ri dec nlf idx inv rrf ohn ohr cnt w w3 tp oht lk m2 we ow gat0 gat1 acc o ost0 ost1
            pool_go pe_go
            g_edges g_prep g_mask g_cnt_mm g_counted g_idx g_rows g_turn_mm g_turned g_lk g_own g_msg
            g_sum_mm g_added g_out g_stored""".split()
        s = {n: sem("s_" + n) for n in names}
        zst = [s["zst0"], s["zst1"]]
        rl = [s["rl0"], s["rl1"]]
        gat = [s["gat0"], s["gat1"]]
        ost = [s["ost0"], s["ost1"]]

        def over_t(ap, n):
            return ap.unsqueeze(2).broadcast_to([ap.shape[0], ap.shape[1], n])

        def over_b(ap, n):
            return ap.unsqueeze(1).broadcast_to([ap.shape[0], n, ap.shape[1]])

        PIECES = [(48, 49, 2, 128), (0, 16, 1, 0), (16, 32, 7, 0), (32, 48, 0, 0)]
        NCOUNT = bank[2][0:NB, 192:193]

        def run_steps(eng, step, last):
            for i in range(4):
                step(i, i % 2)
            with eng.Fori(2, (NB - 1) // 2) as j:
                step(j * 2, 0)
                step(j * 2 + 1, 1)
            for i in range(NB - 1, last + 1):
                step(i, i % 2)

        def dyn(i):
            return not isinstance(i, int)

        block = ctx.enter_context(nc.Block())

        @block.sync
        def _(sp):
            ev = lambda a: a.rearrange("(p c) -> p c", p=EP)
            for k, a in enumerate((src, dst, rel)):
                sp.dma_start(raw[k], ev(a)).then_inc(s["edges_in"], 16)
            sp.dma_start(wload[:, 0, :], tokeys).then_inc(s["w_in"], 16)
            sp.dma_start(wload[:, 1, :], toqueries).then_inc(s["w_in"], 16)
            sp.dma_start(rload[:, 0:EMB], relations).then_inc(s["w_in"], 16)
            sp.dma_start(rload[:, EMB:EMB + NBASE], comps).then_inc(s["w_in"], 16)
            sp.dma_start(bases.rearrange("p h j -> p (h j)"), bases_w.rearrange("b (q h) j -> (b q) (h j)", q=Q)).then_inc(s["bases_in"], 16)
            sp.wait_ge(s["const"], 1)
            sp.dma_start(X[:, 0:NB - 1, :], x[0:(NB - 1) * P, :].rearrange("(b p) i -> p b i", p=P))\
                .then_inc(s["x_in"], 16)
            sp.dma_start(X[0:LASTN, NB - 1, :], x[(NB - 1) * P:N, :]).then_inc(s["x_in"], 16)
            sp.dma_start(Z[N * R:N * R + 1, :], zrow[:, :]).then_inc(s["zrow"], 16)

            def store_z(i, par, n=P):
                sp.wait_ge(s["z_sb"], i * 4 + 4)
                zr = Z[bass.ds(i * (P * R), n * R), :].rearrange("(p r) i -> p (r i)", r=R)
                sp.dma_start(zr, ZS[par][0:n, :]).then_inc(zst[par], 16)

            with sp.Fori(0, (NB - 1) // 2) as j:
                store_z(j * 2, 0)
                store_z(j * 2 + 1, 1)
            store_z(NB - 1, 0, LASTN)

            sp.wait_ge(s["marks_st"], 16)
            sp.wait_ge(s["nt_row"], 1)
            bad = sp.value_load(ROWI[0:1, 3 * NB:3 * NB + 1], min_val=0, max_val=16 * NB)
            with sp.If(bad < 1):
                def bucket(b, par):
                    if dyn(b) or b < NB:
                        if dyn(b) or b >= 2:
                            sp.wait_ge(s["rl_t"], b - 1)
                        sp.dma_start(RL[par][:, :], stream[bass.ds(b * (STRIDE // P), G), :]).then_inc(rl[par], 16)
                    if dyn(b) or b >= 2:
                        store_out(b - 2, par)

                def store_out(b, par, n=P):
                    sp.wait_ge(s["o"], b + 1)
                    sp.dma_start(out[bass.ds(b * P, n), :], O[par][0:n, :]).then_inc(ost[par], 16)

                bucket(0, 0)
                bucket(1, 1)
                with sp.Fori(0, (NB - 1) // 2 - 1) as j:
                    bucket(j * 2 + 2, 0)
                    bucket(j * 2 + 3, 1)
                bucket(NB - 1, 0)
                store_out(NB - 2, 1)
                store_out(NB - 1, 0, LASTN)
                sp.wait_ge(ost[0], 16 * ((NB + 1) // 2))
                sp.wait_ge(ost[1], 16 * (NB // 2))
            with sp.If(bad > 0):
                sp.wait_ge(zst[0], 16 * ((NB + 1) // 2))
                sp.wait_ge(zst[1], 16 * (NB // 2))
                for k, a in enumerate((src, dst, rel)):
                    sp.dma_start(raw[k], ev(a)).then_inc(s["g_edges"], 16)
                sp.wait_ge(s["g_out"], 1)
                sp.dma_start(out[0:(NB - 1) * P, :].rearrange("(b p) i -> p b i", p=P), X[:, 0:NB - 1, :])\
                    .then_inc(s["g_stored"], 16)
                sp.dma_start(out[(NB - 1) * P:N, :], X[0:LASTN, NB - 1, :]).then_inc(s["g_stored"], 16)
                sp.wait_ge(s["g_stored"], 32)
        @block.gpsimd
        def _(pool):
            g = nc.gpsimd
            g.memset(X[:, NB - 1, :], 0.0)
            g.memset(zrow[:, :], 0.0)
            g.drain().then_inc(s["const"], 1)
            g.iota(iotaB[:], [[1, NB], [0, TC]], base=0, channel_multiplier=0, allow_small_or_imprecise_dtypes=True)
            g.iota(iotaS[:], [[1, WIN], [0, TC]], base=1, channel_multiplier=0, allow_small_or_imprecise_dtypes=True)
            g.iota(iotaN[:], [[1, P]], base=0, channel_multiplier=0, allow_small_or_imprecise_dtypes=True)
            g.memset(restart[:], 1.0)
            g.memset(identf[:], 0.0)
            g.memset(ident4k[:], 0.0)
            g.memset(ident16[:], 0.0)
            g.memset(identb[:], 0.0)
            g.memset(before16[:], 1.0)
            g.memset(ones16[:], 1.0)
            g.memset(MX[:], 0.0)
            g.memset(upto16[:], 16.0)
            g.memset(spread[:], 0.0)
            g.iota(QI[:, 0:1], [[0, 1]], base=0, channel_multiplier=1)
            g.iota(PARI[:, 0:1], [[0, 1]], base=0, channel_multiplier=1)
            g.memset(epsc[:], EPS)
            g.iota(POSI[:], [[0, 1]], base=0, channel_multiplier=STRIDE)
            g.drain().then_inc(s["const"], 1)
            pool.wait_ge(s["const"], 2)
            g.tensor_copy(POS[:, 0:1], POSI[:])
            g.memset(restart[:, :, 0:1], 0.0)
            for t, fill in ((identf, 1.0), (ident4k, 4096.0), (ident16, 1.0), (identb, 1.0)):
                g.affine_select(out=t[:], in_=t[:], compare_op=ALU.not_equal, fill=fill, base=0,
                                pattern=[[-1, P]], channel_multiplier=1)
            g.affine_select(out=spread[:], in_=spread[:], compare_op=ALU.not_equal, fill=1.0, base=0,
                            pattern=[[1, NBASE], [0, Q]], channel_multiplier=-1)
            g.affine_select(out=before16[:], in_=before16[:], compare_op=ALU.is_gt, fill=0.0, base=0,
                            pattern=[[1, EP]], channel_multiplier=-1)
            g.affine_select(out=upto16[:], in_=upto16[:], compare_op=ALU.is_ge, fill=0.0, base=0,
                            pattern=[[1, NB]], channel_multiplier=-1)
            g.drain().then_inc(s["const"], 1)
            pool.wait_ge(s["const"], 3)
            g.tensor_scalar_add(LIM[:], POS[:, 0:1], float(BCAP)).then_inc(s["const"], 1)

            def scatter(i, par):
                pool.wait_ge(s["rec_sb"], i + 1)
                pool.wait_ge(s["idxw"], i + 1)
                if dyn(i) or i >= 1:
                    pool.wait_ge(s["scat"], i * 16)
                pool.sem_inc(s["pool_go"], 1)
                g.indirect_dma_start(stream, bass.IndirectOffsetOnAxis(IDXW[par][:, 0:1], 1), REC[par][:], None)\
                    .then_inc(s["scat"], 16)

            def key_query(i, par):
                pool.wait_ge(s["so_sb"], i + 1)
                if dyn(i) or i >= 2:
                    pool.wait_ge(s["rec_mm"], i - 1)
                g.tensor_tensor(PR[par][:], SO[:, 0:P], SO[:, P:2 * P], ALU.mult).then_inc(s["prod"], 1)

            def step(i, par):
                if dyn(i) or 1 <= i <= NB:
                    key_query(i - 1, 1 - par)
                if dyn(i) or 2 <= i:
                    scatter(i - 2, par)

            run_steps(pool, step, NCH + 1)
            g.memset(marks, float(SENT)).then_inc(s["marks_sb"], 1)
            pool.wait_ge(s["marks_sb"], 1)
            pool.wait_ge(s["idxw"], NCH + 1)
            pool.wait_ge(s["scat"], NCH * 16)
            g.indirect_dma_start(stream.rearrange("(a k) p -> a (k p)", k=G),
                                 bass.IndirectOffsetOnAxis(IDXW[NCH % 2][:, 0:1], 1), marks, None)\
                .then_inc(s["marks_st"], 16)

            pool.wait_ge(zst[0], 16 * ((NB + 1) // 2))
            pool.wait_ge(zst[1], 16 * (NB // 2))
            pool.wait_ge(s["zrow"], 16)
            pool.wait_ge(s["nt_row"], 1)

            bad = pool.value_load(ROWI[0:1, 3 * NB:3 * NB + 1], min_val=0, max_val=16 * NB)
            with pool.If(bad < 1):
                def gather(b, par):
                    n = pool.value_load(ROWI[0:1, bass.ds(b, 1)], min_val=1, max_val=G)
                    pool.wait_ge(s["idx"], b + 1)
                    if dyn(b) or b >= 2:
                        pool.wait_ge(s["acc"], b - 1)

                    pool.sem_inc(s["pool_go"], 1)

                    def tile(k):
                        g.indirect_dma_start(Gbuf[par][:, k, :], None, Z, bass.IndirectOffsetOnAxis(IDX[par][:, k:k + 1], 0))\
                            .then_inc(gat[par], 16)
                        if k + 1 < G:
                            with pool.If(n > k + 1):
                                tile(k + 1)
                    tile(0)

                for p in range(2):
                    g.memset(Gbuf[p], 0.0).then_inc(s["marks_sb"], 1)
                pool.wait_ge(s["marks_sb"], 3)
                gather(0, 0)
                gather(1, 1)
                with pool.Fori(1, (NB - 1) // 2) as j:
                    gather(j * 2, 0)
                    gather(j * 2 + 1, 1)
                gather(NB - 1, 0)
            with pool.If(bad > 0):
                with pool.Fori(0, NCOL) as t:
                    pool.wait_ge(s["g_idx"], t + 1)
                    pool.sem_inc(s["pool_go"], 1)
                    g.indirect_dma_start(gen_rows, None, Z, bass.IndirectOffsetOnAxis(gen_idx, 0))\
                        .then_inc(s["g_rows"], 16)
        @block.vector
        def _(dve):
            v = nc.vector
            cnt = {}

            def chain(ins, name):
                cnt[name] = cnt.get(name, 0) + 1
                ins.then_inc(s[name], 1)
                dve.wait_ge(s[name], cnt[name])

            dve.wait_ge(s["edges_in"], 48)
            SRC, DST, REL, A, B = raw
            chain(v.tensor_scalar(A, SRC, 7, None, ALU.logical_shift_right), "edge")
            v.tensor_copy(q16[:], A).then_inc(s["edges_done"], 1)
            chain(v.tensor_scalar(B, SRC, 127, None, ALU.bitwise_and), "edge")
            chain(v.tensor_scalar(SRC, DST, 1, None, ALU.logical_shift_right), "edge")
            v.tensor_scalar(hi16[:], SRC, BIG, None, ALU.subtract).then_inc(s["edges_done"], 1)
            dve.wait_ge(s["edges_done"], 2)
            chain(v.tensor_scalar(A, REL, 7, None, ALU.logical_shift_left), "edge")
            chain(v.tensor_tensor(B, A, B, ALU.bitwise_or), "edge")
            chain(v.tensor_scalar(A, DST, 1, 11, ALU.bitwise_and, ALU.logical_shift_left), "edge")
            chain(v.tensor_tensor(B, A, B, ALU.bitwise_or), "edge")
            v.tensor_scalar(lo16[:], B, BIG, None, ALU.subtract).then_inc(s["edges_done"], 1)
            dve.wait_ge(s["edges_done"], 3)

            dve.wait_ge(s["const"], 4)
            chain(v.tensor_scalar(QI[:, 1:2], QI[:, 0:1], Q - 1, None, ALU.bitwise_and), "edge")
            chain(v.tensor_copy(stats[:, 0, 0:1], QI[:, 1:2]), "edge")
            chain(v.tensor_scalar(qmask[:], iotaN[:, 0:Q], stats[:, 0, 0:1], None, ALU.is_equal), "edge")
            dve.wait_ge(s["kq_t"], 3)
            chain(v.tensor_copy(compsB[:], bank[5][:, 128:128 + R]), "edge")
            v.tensor_tensor(compsD[:], over_t(qmask[:], R), over_b(compsB[:], Q), ALU.mult).then_inc(s["comps_d"], 1)

            dve.wait_ge(s["x_in"], 32)
            for b in range(NB):
                v.bn_stats(stats[:, b, :], X[:, b, :]).then_inc(s["stat"], 1)
            for b in range(NB):
                dve.wait_ge(s["stat"], b + 1)
                v.bn_aggr(mv[:, b, :], stats[:, b, :]).then_inc(s["varr"], 1)
            for k in range(4):
                dve.wait_ge(s["wt_mm"], k + 1)
                for h in range(4):
                    v.tensor_copy(WT[:].rearrange("p r (q h) -> p h q r", q=Q)[:, 4 * k + h, :, :],
                                  bank[k][:, h * Q * R:(h + 1) * Q * R].rearrange("p (q r) -> p q r", r=R))\
                        .then_inc(s["wt_sb"], 1)
            dve.wait_ge(s["stdd"], 1)
            v.reciprocal(rstd[:], std[:]).then_inc(s["ln"], 1)
            dve.wait_ge(s["ln"], 1)

            def bucket_onehot(i, par):
                if dyn(i) or i >= 2:
                    dve.wait_ge(s["m_sum"], i - 1)
                v.tensor_tensor(OHB[par][:], iotaB[:], over_b(q16[:, bass.ds(i * TC, TC)], NB), ALU.is_equal)\
                    .then_inc(s["ohb"], 1)
                dve.wait_ge(s["ohb"], i + 1)
                if dyn(i) or i >= 2:
                    dve.wait_ge(s["pf"], i * 4 - 4)
                v.tensor_tensor_scan(SC[par][:].rearrange("p b t -> p (b t)"),
                                     restart[:].rearrange("p b t -> p (b t)"),
                                     OHB[par][:].rearrange("p b t -> p (b t)"), 0.0, ALU.mult, ALU.add)\
                    .then_inc(s["scan"], 1)

            def payload(i, par):
                if dyn(i) or i >= 2:
                    dve.wait_ge(s["d_mm"], i - 1)
                for k, half in enumerate((hi16, lo16)):
                    v.tensor_tensor(PAY[par][:, k, :, :], OHB[par][:], over_b(half[:, bass.ds(i * TC, TC)], NB), ALU.mult)\
                        .then_inc(s["pay"], 1)

            def chunk_counts(i, par):
                dve.wait_ge(s["ncount"], i + 1)
                if dyn(i) or i >= 1:
                    dve.wait_ge(s["mx"], i)
                    dve.wait_ge(s["pos"], i)
                v.tensor_tensor(MX[:], COUNT[par][:], MX[:], ALU.max).then_inc(s["mx"], 1)
                v.scalar_tensor_tensor(out=POS[:, bass.ds(i + 1, 1)], in0=COUNT[par][:], scalar=POS[:, bass.ds(i, 1)],
                                       in1=LIM[:], op0=ALU.add, op1=ALU.min).then_inc(s["pos"], 1)

            def ranks(i, par):
                dve.wait_ge(s["pfread"], i * 4 + 4)
                if dyn(i) or i >= 1:
                    dve.wait_ge(s["m_sum"], i)
                v.tensor_tensor(M[:], PFS[:], OHB[par][:], ALU.mult).then_inc(s["own"], 1)
                dve.wait_ge(s["own"], i + 1)
                if dyn(i) or i >= 1:
                    dve.wait_ge(s["ohs"], i)
                with nc.allow_low_precision("whole numbers"):
                    v.tensor_reduce(RK16[:], M[:].rearrange("p b t -> p t b"), AX.X, ALU.add).then_inc(s["m_sum"], 1)
                dve.wait_ge(s["m_sum"], i + 1)
                if dyn(i) or i >= 2:
                    dve.wait_ge(s["d_mm"], i - 1)
                v.tensor_tensor(OHS[par][:], iotaS[:], over_b(RK16[:], WIN), ALU.is_equal).then_inc(s["ohs"], 1)

            def normalise(i):
                if dyn(i) or i >= 1:
                    dve.wait_ge(s["th"], i)
                v.tensor_scalar(H[:], X[:, bass.ds(i, 1), :].rearrange("p a i -> p (a i)"), mv[:, bass.ds(i, 1), 0],
                                rstd[:, bass.ds(i, 1)], ALU.subtract, ALU.mult).then_inc(s["h"], 1)

            def window_index(i, par):
                if dyn(i) or i >= 2:
                    dve.wait_ge(s["scat"], i * 16 - 16)
                v.tensor_copy(IDXW[par][:], POS[:, bass.ds(i, 1)]).then_inc(s["idxw"], 1)

            def step(i, par):
                if dyn(i) or 2 <= i:
                    window_index(i - 2, par)
                if dyn(i) or i < NB:
                    normalise(i)
                if dyn(i) or i < NCH:
                    chunk_counts(i, par)
                if dyn(i) or i + 1 < NCH:
                    bucket_onehot(i + 1, 1 - par)
                if dyn(i) or i < NCH:
                    payload(i, par)
                if dyn(i) or i < NCH:
                    ranks(i, par)

            dve.wait_ge(s["varr"], NB)
            bucket_onehot(0, 0)
            run_steps(dve, step, NCH + 1)

            dve.wait_ge(s["pos"], NCH)
            dve.wait_ge(s["scat"], NCH * 16 - 16)
            v.tensor_copy(IDXW[NCH % 2][:], POS[:, NCH:NCH + 1]).then_inc(s["idxw"], 1)
            dve.wait_ge(s["mx"], NCH)
            chain(v.tensor_tensor(NT[:, 0:1], POS[:, NCH:NCH + 1], POS[:, 0:1], ALU.subtract), "nt")
            chain(v.tensor_scalar(NTI[:, 0:1], NT[:, 0:1], float(P - 1), None, ALU.add), "nt")
            chain(v.tensor_scalar(NTI[:, 1:2], NTI[:, 0:1], 7, None, ALU.logical_shift_right), "nt")
            chain(v.tensor_scalar(NT[:, 1:2], NTI[:, 1:2], 1.0, None, ALU.max), "nt")
            chain(v.tensor_scalar(PARI[:, 1:2], PARI[:, 0:1], 1, None, ALU.bitwise_and), "nt")
            chain(v.tensor_tensor(NT[:, 3:4], NT[:, 1:2], PARI[:, 1:2], ALU.mult), "nt")
            chain(v.tensor_tensor(NT[:, 2:3], NT[:, 1:2], NT[:, 3:4], ALU.subtract), "nt")
            chain(v.tensor_scalar(NT[:, 4:5], MX[:], float(WIN), None, ALU.is_gt), "nt")
            chain(v.tensor_scalar(NT[:, 5:6], NT[:, 0:1], float(BCAP), None, ALU.is_ge), "nt")
            chain(v.tensor_tensor(NT[:, 4:5], NT[:, 4:5], NT[:, 5:6], ALU.max), "nt")
            dve.wait_ge(s["nt_mm"], 1)
            v.tensor_copy(ROWI[:], bank[3][0:1, 0:3 * NB + 1]).then_inc(s["nt_row"], 1)

            dve.wait_ge(s["nt_row"], 1)
            bad = dve.value_load(ROWI[0:1, 3 * NB:3 * NB + 1], min_val=0, max_val=16 * NB)
            with dve.If(bad < 1):
                def tables(b, par):
                    dve.wait_ge(s["rl_t"], b + 1)
                    if dyn(b) or b >= 1:
                        dve.wait_ge(s["dec"], b * 2)
                    v.tensor_copy(RI[:], bank[3][:, 0:G]).then_inc(s["ri"], 1)
                    dve.wait_ge(s["ri"], b + 1)
                    if dyn(b) or b >= 2:
                        dve.wait_ge(s["acc"], b - 1)
                    v.tensor_scalar(IDX[par][:], RI[:], 7, None, ALU.logical_shift_right).then_inc(s["idx"], 1)
                    if dyn(b) or b >= 1:
                        dve.wait_ge(s["rrf"], b)
                    v.tensor_scalar(NLI[:, 0, :], RI[:], 127, None, ALU.bitwise_and).then_inc(s["dec"], 1)
                    v.tensor_scalar(NLI[:, 1, :], RI[:], 7, R - 1, ALU.logical_shift_right, ALU.bitwise_and)\
                        .then_inc(s["dec"], 1)
                    v.tensor_scalar(INV[:], RI[:], float(SENT), float(R), ALU.is_ge, ALU.mult).then_inc(s["inv"], 1)
                    dve.wait_ge(s["dec"], b * 2 + 2)
                    dve.wait_ge(s["inv"], b + 1)
                    if dyn(b) or b >= 1:
                        dve.wait_ge(s["ohn"], b)
                        dve.wait_ge(s["ohr"], b)
                    v.tensor_copy(NLF[:], NLI[:, 0, :]).then_inc(s["nlf"], 1)
                    v.tensor_tensor(RRF[:], NLI[:, 1, :], INV[:], ALU.add).then_inc(s["rrf"], 1)
                    dve.wait_ge(s["nlf"], b + 1)
                    dve.wait_ge(s["rrf"], b + 1)
                    v.tensor_tensor(OHR[par][:], over_b(iotaN[:, 0:R], G), over_t(RRF[:], R), ALU.is_equal)\
                        .then_inc(s["ohr"], 1)
                    v.tensor_tensor(OHN[par], over_b(iotaN[:], G), over_t(NLF[:], P), ALU.is_equal)\
                        .then_inc(s["ohn"], 1)

                def weights(b, par):
                    dve.wait_ge(s["cnt"], b + 1)
                    vb = V[:, bass.ds(b, 1), :].rearrange("p a r -> p (a r)")
                    base = 7 * b
                    def link(ins, k):
                        ins.then_inc(s["w"], 1)
                        dve.wait_ge(s["w"], base + k)
                    link(v.tensor_scalar(WC[:, 0, :], bank[4][:, 0:R], 1.0, None, ALU.max), 1)
                    link(v.tensor_tensor(WC[:, 1, :], WC[:, 0, :], vb, ALU.mult), 2)
                    link(v.reciprocal(WC[:, 2, :], WC[:, 1, :]), 3)
                    link(v.tensor_tensor(WC[:, 3, :], WC[:, 2, :], vb, ALU.mult), 4)
                    if dyn(b) or b >= 1:
                        dve.wait_ge(s["lk"], 4 * b)
                    link(v.tensor_copy(W3[:, 0, :], WC[:, 3, :]), 5)
                    link(v.tensor_tensor(WC[:, 4, :], WC[:, 3, :], W3[:, 0, :], ALU.subtract), 6)
                    link(v.tensor_copy(W3[:, 1, :], WC[:, 4, :]), 7)
                    v.tensor_tensor(W3[:, 2, :], WC[:, 4, :], W3[:, 1, :], ALU.subtract).then_inc(s["w3"], 1)

                def edge_weights(b, par):
                    for k in range(4):
                        dve.wait_ge(s["lk"], b * 4 + k + 1)
                        if dyn(b) or b >= 1 or k >= 1:
                            dve.wait_ge(s["we"], b * 4 + k)
                        lk = bank[k % 2][:, 0:9 * 3 * R].rearrange("p (k x r) -> p k x r", x=3, r=R)
                        oh = OHR[par][:, 9 * k:9 * k + 9, :].unsqueeze(2).broadcast_to([P, 9, 3, R])
                        v.tensor_tensor(M2[:], lk, oh, ALU.mult).then_inc(s["m2"], 1)
                        dve.wait_ge(s["m2"], b * 4 + k + 1)
                        v.tensor_reduce(WE[par][:, 9 * k:9 * k + 9], M2[:].rearrange("p k x r -> p k (x r)"), AX.X, ALU.add)\
                            .then_inc(s["we"], 1)

                def weighted_onehot(b, par):
                    dve.wait_ge(s["we"], b * 4 + 4)
                    if dyn(b) or b >= 1:
                        dve.wait_ge(s["acc"], b)
                    v.tensor_tensor(OW, OHN[par], over_t(WE[par][:], P), ALU.mult).then_inc(s["ow"], 1)

                def finish(b, par):
                    dve.wait_ge(s["acc"], b + 1)
                    if dyn(b) or b >= 2:
                        dve.wait_ge(ost[par], out_total(b))
                    v.scalar_tensor_tensor(out=O[par][:], in0=bank[(2, 5)[par]][:, 0:EMB], scalar=0.0,
                                           in1=X[:, bass.ds(b, 1), :].rearrange("p a i -> p (a i)"), op0=ALU.max, op1=ALU.add)\
                        .then_inc(s["o"], 1)

                def stepb(b, par, o_total):
                    stored["o"] = o_total
                    if dyn(b) or b < NB:
                        tables(b, par)
                        weights(b, par)
                        edge_weights(b, par)
                    if dyn(b) or 1 <= b <= NB:
                        weighted_onehot(b - 1, 1 - par)
                    if dyn(b) or 2 <= b <= NB + 1:
                        finish(b - 2, par)

                stored = {}
                out_total = lambda b: stored["o"]
                for p in range(2):
                    dve.wait_ge(zst[p], 16 * ((NB + 1 - p) // 2))
                for b in range(4):
                    stepb(b, b % 2, 0)
                with dve.Fori(2, (NB - 1) // 2) as j:
                    stepb(j * 2, 0, j * 16 - 16)
                    stepb(j * 2 + 1, 1, j * 16 - 16)
                for b in (NB - 1, NB, NB + 1):
                    stepb(b, b % 2, (b // 2 - 1) * 16)
            with dve.If(bad > 0):
                dve.wait_ge(s["marks_st"], 16)
                dve.wait_ge(s["g_edges"], 48)
                chain(v.tensor_scalar(raw[3], raw[0], P - 1, None, ALU.bitwise_and), "g_prep")
                chain(v.tensor_copy(gen_nloc, raw[3]), "g_prep")
                chain(v.tensor_scalar(raw[4], raw[1], 4, None, ALU.logical_shift_left), "g_prep")
                chain(v.tensor_tensor(raw[3], raw[4], raw[2], ALU.bitwise_or), "g_prep")
                chain(v.tensor_copy(gen_rel, raw[2]), "g_prep")
                chain(v.memset(gen_cnt, 0.0), "g_prep")
                chain(v.memset(gen_acc, 0.0), "g_prep")
                dve.sem_inc(s["g_counted"], 2)
                dve.sem_inc(s["g_added"], 2)

                def masks(t, base):
                    v.tensor_scalar(gen_node, iotaN[0:EP, :], gen_nloc[:, bass.ds(t, 1)], None, ALU.is_equal)\
                        .then_inc(s["g_mask"], 1)
                    v.tensor_tensor(gen_bucket, iotaB[:, :, 0], q16[:, bass.ds(t, 1)].broadcast_to([EP, NB]), ALU.is_equal)\
                        .then_inc(s["g_mask"], 1)
                    v.tensor_scalar(gen_r, iotaN[0:EP, 0:R], gen_rel[:, bass.ds(t, 1)], None, ALU.is_equal)\
                        .then_inc(s["g_mask"], 1)
                    dve.wait_ge(s["g_mask"], base + 3)
                    v.tensor_tensor(gen_br, over_t(gen_bucket, R), over_b(gen_r, NB), ALU.mult).then_inc(s["g_mask"], 1)
                    dve.wait_ge(s["g_mask"], base + 4)

                with dve.Fori(0, NCOL) as t:
                    masks(t, t * 4)
                    dve.wait_ge(s["g_cnt_mm"], t + 1)
                    for k in range(2):
                        v.tensor_tensor(gen_cnt_half[k], gen_cnt_half[k], bank[k][:, 0:HALF], ALU.add)\
                            .then_inc(s["g_counted"], 1)
                    dve.wait_ge(s["g_counted"], t * 2 + 4)
                gen_v = V[:].rearrange("p b r -> p (b r)")
                chain(v.tensor_scalar(gen_cnt, gen_cnt, 1.0, None, ALU.max), "g_prep")
                chain(v.tensor_tensor(gen_cnt, gen_cnt, gen_v, ALU.mult), "g_prep")
                chain(v.reciprocal(gen_w, gen_cnt), "g_prep")
                chain(v.tensor_tensor(gen_w, gen_w, gen_v, ALU.mult), "g_prep")

                with dve.Fori(0, NCOL) as t:
                    v.tensor_copy(gen_idx, raw[3][:, bass.ds(t, 1)]).then_inc(s["g_idx"], 1)
                    masks(t, t * 4 + 4 * NCOL)
                    dve.wait_ge(s["g_lk"], t + 1)
                    for k in range(2):
                        v.tensor_tensor(gen_picked[:, k * HALF:(k + 1) * HALF], bank[k][0:EP, 0:HALF],
                                        gen_br_flat[:, k * HALF:(k + 1) * HALF], ALU.mult).then_inc(s["g_own"], 1)
                    dve.wait_ge(s["g_own"], t * 4 + 2)
                    v.tensor_reduce(gen_we, gen_picked, AX.X, ALU.add).then_inc(s["g_own"], 1)
                    dve.wait_ge(s["g_own"], t * 4 + 3)
                    v.tensor_scalar(gen_bw, gen_bucket, gen_we, None, ALU.mult).then_inc(s["g_own"], 1)
                    dve.wait_ge(s["g_own"], t * 4 + 4)
                    dve.wait_ge(s["g_rows"], t * 16 + 16)
                    v.tensor_tensor(gen_msg, over_t(gen_bw, EMB), over_b(gen_rows, NB), ALU.mult).then_inc(s["g_msg"], 1)
                    for k in range(GCH):
                        dve.wait_ge(s["g_sum_mm"], t * GCH + k + 1)
                        n = min(512, NB * EMB - k * 512)
                        part = gen_acc[:, k * 512:k * 512 + n]
                        v.tensor_tensor(part, part, bank[2 + k % 2][:, 0:n], ALU.add).then_inc(s["g_added"], 1)
                    dve.wait_ge(s["g_added"], t * GCH + GCH + 2)
                v.scalar_tensor_tensor(out=X[:].rearrange("p b i -> p (b i)"), in0=gen_acc, scalar=0.0,
                                       in1=X[:].rearrange("p b i -> p (b i)"), op0=ALU.max, op1=ALU.add)\
                    .then_inc(s["g_out"], 1)
        @block.scalar
        def _(act):
            a = nc.scalar
            act.wait_ge(s["kq_t"], 1)
            a.copy(KQT[:].rearrange("p x k -> p (x k)"), bank[4][:, 0:256]).then_inc(s["kq_sb"], 1)
            act.wait_ge(s["kq_t"], 2)
            a.copy(relT[:], bank[5][:, 0:R]).then_inc(s["kq_sb"], 1)
            a.copy(compsT[:], bank[5][0:NBASE, 64:64 + R]).then_inc(s["kq_sb"], 1)
            act.wait_ge(s["varr"], NB)
            act.wait_ge(s["const"], 4)
            a.activation(std[:], mv[:, :, 1], ACT.Sqrt, bias=epsc[:, 0:1]).then_inc(s["stdd"], 1)
            act.wait_ge(s["edges_done"], 3)

            def relu_ht(i, par):
                act.wait_ge(s["th"], i + 1)
                if dyn(i) or i >= 2:
                    act.wait_ge(s["z_mm"], i * 4 - 4)
                a.activation(HT[par][:], bank[6][:, 0:P], ACT.Relu).then_inc(s["ht"], 1)

            def copy_prefix(i, par):
                for k, (b0, b1, pb, c0) in enumerate(PIECES):
                    act.wait_ge(s["pf"], i * 4 + k + 1)
                    if k == 0:
                        if dyn(i) or i >= 2:
                            act.wait_ge(s["mx"], i - 1)
                            act.wait_ge(s["pos"], i - 1)
                        a.copy(COUNT[par][:], NCOUNT).then_inc(s["ncount"], 1)
                        if dyn(i) or i >= 1:
                            act.wait_ge(s["own"], i)
                    a.copy(PFS[:, b0:b1, :].rearrange("p b t -> p (b t)"), bank[pb][0:EP, c0:c0 + (b1 - b0) * TC])\
                        .then_inc(s["pfread"], 1)

            def copy_so(i):
                act.wait_ge(s["so_mm"], i + 1)
                if dyn(i) or i >= 1:
                    act.wait_ge(s["prod"], i)
                a.copy(SO[:], bank[6][:, 0:2 * P]).then_inc(s["so_sb"], 1)

            def copy_d(i, par):
                act.wait_ge(s["d_mm"], i + 1)
                if dyn(i) or i >= 2:
                    act.wait_ge(s["rec_mm"], i - 1)
                a.copy(DS[par][:], bank[2][:, 0:2 * NB]).then_inc(s["d_sb"], 1)

            def copy_rec(i, par):
                act.wait_ge(s["rec_mm"], i + 1)
                if dyn(i) or i >= 2:
                    act.wait_ge(s["scat"], i * 16 - 16)
                a.activation(REC[par][:], bank[3][0:NB, 0:WIN], ACT.Copy, bias=BIG * 4097).then_inc(s["rec_sb"], 1)
                if dyn(i) or i < NB:
                    a.activation(V[:, bass.ds(i, 1), :].rearrange("p a r -> p (a r)"), bank[3][:, 256:256 + R],
                                 ACT.Exp, scale=1.0 / EMB).then_inc(s["v"], 1)
                else:
                    a.copy(stats[0:1, 0, 0:1], stats[0:1, 0, 1:2]).then_inc(s["v"], 1)

            def copy_z(i, par):
                for k in range(4):
                    act.wait_ge(s["z_mm"], i * 4 + k + 1)
                    if k == 0 and (dyn(i) or i >= 2):
                        act.wait_ge(zst[par], z_total(i))
                    a.copy(ZS[par][:, k * 512:(k + 1) * 512], bank[4 + k % 2][:, :]).then_inc(s["z_sb"], 1)

            tot = {}
            z_total = lambda i: tot["z"]

            def step(i, par, zt):
                tot["z"] = zt
                if dyn(i) or i < NCH:
                    copy_prefix(i, par)
                if dyn(i) or i < NB:
                    relu_ht(i, par)
                if dyn(i) or 1 <= i <= NCH:
                    copy_d(i - 1, 1 - par)
                if dyn(i) or i < NB:
                    copy_so(i)
                    copy_z(i, par)
                if dyn(i) or 2 <= i:
                    copy_rec(i - 2, par)

            for i in range(4):
                step(i, i % 2, (i // 2) * 16)
            with act.Fori(2, (NB - 1) // 2) as j:
                step(j * 2, 0, j * 16)
                step(j * 2 + 1, 1, j * 16)
            for i in range(NB - 1, NCH + 2):
                step(i, i % 2, (i // 2) * 16)

            act.wait_ge(s["nt_row"], 1)
            bad = act.value_load(ROWI[0:1, 3 * NB:3 * NB + 1], min_val=0, max_val=16 * NB)
            with act.If(bad < 1):
                def bucket(b, par):
                    for k in range(5):
                        act.wait_ge(s["tp"], b * 5 + k + 1)
                        if k == 0 and (dyn(b) or b >= 1):
                            act.wait_ge(s["lk"], b * 4)
                        n = min(8, G - 8 * k)
                        a.copy(OHT[:, 8 * k:8 * k + n, :].rearrange("p k e -> p (k e)"),
                               bank[6 + k % 2][:, :].bitcast(BF16)[:, 0:n * P]).then_inc(s["oht"], 1)

                bucket(0, 0)
                bucket(1, 1)
                with act.Fori(1, (NB - 1) // 2) as j:
                    bucket(j * 2, 0)
                    bucket(j * 2 + 1, 1)
                bucket(NB - 1, 0)
            with act.If(bad > 0):
                with act.Fori(0, NCOL) as t:
                    act.wait_ge(s["g_turn_mm"], t + 1)
                    a.copy(gen_nodeT, bank[6][:, 0:EP]).then_inc(s["g_turned"], 1)
        @block.tensor
        def _(pe):
            t_ = nc.tensor
            pe.wait_ge(s["const"], 4)
            pe.wait_ge(s["w_in"], 64)
            t_.transpose(bank[4][:, 0:P], wload[:, 0, :], identf[:])
            t_.transpose(bank[4][:, P:2 * P], wload[:, 1, :], identf[:]).then_inc(s["kq_t"], 1)
            t_.transpose(bank[5][:, 0:R], rload[:, 0:EMB], identf[0:R, 0:R])
            t_.transpose(bank[5][0:NBASE, 64:64 + R], rload[:, EMB:EMB + NBASE], identf[0:R, 0:R])\
                .then_inc(s["kq_t"], 1)
            pe.wait_ge(s["kq_sb"], 3)
            pe.wait_ge(s["bases_in"], 16)
            t_.matmul(bank[5][:, 128:128 + R], spread[:].rearrange("p b q -> p (b q)"), compsT[:], start=True, stop=True)\
                .then_inc(s["kq_t"], 1)
            pe.wait_ge(s["comps_d"], 1)
            for h in range(EMB // Q):
                mm = t_.matmul(bank[h // 4][:, (h % 4) * Q * R:(h % 4 + 1) * Q * R], bases[:, h, :],
                               compsD[:].rearrange("p q r -> p (q r)"), start=(h % 4 == 0), stop=True, skip_group_check=True)
                if h % 4 == 3:
                    mm.then_inc(s["wt_mm"], 1)
            pe.wait_ge(s["wt_sb"], 16)

            def prefix(i, par):
                pe.wait_ge(s["scan"], i + 1)
                if dyn(i) or i >= 1:
                    pe.wait_ge(s["ncount"], i)
                if dyn(i) or i >= 2:
                    pe.wait_ge(s["d_sb"], i - 1)
                t_.matmul(NCOUNT, SC[par][:, :, TC - 1], ones16[:], start=True, stop=True)
                for k, (b0, b1, pb, c0) in enumerate(PIECES):
                    if dyn(i) or i >= 1:
                        pe.wait_ge(s["pfread"], i * 4 - 3 + k)
                    o = bank[pb][0:EP, c0:c0 + (b1 - b0) * TC]
                    t_.matmul(o, before16[:], over_t(SC[par][:, b0:b1, TC - 1], TC), start=True, stop=False)
                    t_.matmul(o, ident16[0:EP, 0:EP], SC[par][:, b0:b1, :].rearrange("p b t -> p (b t)"),
                              start=False, stop=True).then_inc(s["pf"], 1)

            def transpose_h(i):
                pe.wait_ge(s["h"], i + 1)
                if dyn(i) or i >= 1:
                    pe.wait_ge(s["so_sb"], i)
                t_.transpose(bank[6][:, 0:P], H[:], identf[:]).then_inc(s["th"], 1)

            def compact(i, par):
                pe.wait_ge(s["ohs"], i + 1)
                pe.wait_ge(s["pay"], i * 2 + 2)
                if dyn(i) or i >= 1:
                    pe.wait_ge(s["d_sb"], i)
                if dyn(i) or i + 1 < NCH:
                    pe.wait_ge(s["pfread"], i * 4 + 5)
                    pe.wait_ge(s["ncount"], i + 2)
                for t in range(TC):
                    mm = t_.matmul(bank[2][:, 0:2 * NB], OHS[par][:, :, t],
                                   PAY[par][:, :, :, t].rearrange("p x b -> p (x b)"),
                                   start=(t == 0), stop=(t == TC - 1))
                mm.then_inc(s["d_mm"], 1)

            def keys_queries(i, par):
                pe.wait_ge(s["ht"], i + 1)
                t_.matmul(bank[6][:, 0:P], KQT[:, 0, :], HT[par][:], start=True, stop=True)
                t_.matmul(bank[6][:, P:2 * P], KQT[:, 1, :], HT[par][:], start=True, stop=True)\
                    .then_inc(s["so_mm"], 1)

            def messages(i, par):
                for k in range(4):
                    if dyn(i) or i >= 1 or k >= 2:
                        pe.wait_ge(s["z_sb"], i * 4 + k - 1)
                    t_.matmul(bank[4 + k % 2][:, :], HT[par][:], WT[:, 4 * k:4 * k + 4, :].rearrange("p r i -> p (r i)"),
                              start=True, stop=True).then_inc(s["z_mm"], 1)

            def records(i, par):
                pe.wait_ge(s["d_sb"], i + 1)
                if dyn(i) or i >= 1:
                    pe.wait_ge(s["rec_sb"], i)
                    pe.wait_ge(s["v"], i)
                if dyn(i) or i < NB:
                    pe.wait_ge(s["prod"], i + 1)
                    t_.matmul(bank[3][:, 256:256 + R], PR[par][:], relT[:], start=True, stop=True)
                t_.matmul(bank[3][0:NB, 0:WIN], DS[par][:, 0:NB], ident4k[:], start=True, stop=False)
                t_.matmul(bank[3][0:NB, 0:WIN], DS[par][:, NB:2 * NB], identf[:], start=False, stop=True)\
                    .then_inc(s["rec_mm"], 1)

            def step(i, par):
                if dyn(i) or i < NCH:
                    prefix(i, par)
                if dyn(i) or i < NB:
                    transpose_h(i)
                if dyn(i) or 1 <= i <= NCH:
                    compact(i - 1, 1 - par)
                if dyn(i) or i < NB:
                    keys_queries(i, par)
                    messages(i, par)
                if dyn(i) or 2 <= i:
                    records(i - 2, par)

            run_steps(pe, step, NCH + 1)
            pe.wait_ge(s["rec_sb"], NCH)
            pe.wait_ge(s["v"], NCH)
            pe.wait_ge(s["nt"], 10)
            t_.matmul(bank[3][0:1, 0:NB], NT[:, 1:2], identf[0:NB, 0:NB], start=True, stop=True)
            for p in range(2):
                t_.matmul(bank[3][0:1, (1 + p) * NB:(2 + p) * NB], NT[:, 2 + p:3 + p], upto16[:], start=True, stop=True)
            t_.matmul(bank[3][0:1, 3 * NB:3 * NB + 1], NT[:, 4:5], upto16[:, NB - 1:NB], start=True, stop=True)\
                .then_inc(s["nt_mm"], 1)
            pe.wait_ge(s["nt_row"], 1)

            bad = pe.value_load(ROWI[0:1, 3 * NB:3 * NB + 1], min_val=0, max_val=16 * NB)
            with pe.If(bad < 1):
                def tables(b, par, rl_total):
                    pe.wait_ge(rl[par], rl_total)
                    if dyn(b) or b >= 1:
                        pe.wait_ge(s["ri"], b)
                    pe.sem_inc(s["pe_go"], 1)
                    t_.transpose(bank[3][:, 0:G], RL[par][:], identf[0:G, 0:G]).then_inc(s["rl_t"], 1)
                    pe.wait_ge(s["ohn"], b + 1)
                    pe.wait_ge(s["ohr"], b + 1)
                    if dyn(b) or b >= 1:
                        pe.wait_ge(s["w"], b * 7)
                    for k in range(G):
                        mm = t_.matmul(bank[4][:, 0:R], OHN[par][:, k, :], OHR[par][:, k, :], start=(k == 0), stop=(k == G - 1))
                    mm.then_inc(s["cnt"], 1)
                    for k in range(5):
                        if dyn(b) or b >= 1 or k >= 2:
                            pe.wait_ge(s["oht"], b * 5 + k - 1)
                        n = min(8, G - 8 * k)
                        for m in range(n):
                            mm = t_.transpose(bank[6 + k % 2][:, :].bitcast(BF16)[:, m * P:(m + 1) * P],
                                              OHN[par][:, 8 * k + m, :], identb[:])
                        mm.then_inc(s["tp"], 1)
                    pe.wait_ge(s["w3"], b + 1)
                    pe.wait_ge(s["oht"], b * 5 + 5)
                    for k in range(4):
                        if dyn(b) or b >= 1 or k >= 2:
                            pe.wait_ge(s["m2"], b * 4 + k - 1)
                        for m in range(9):
                            mm = t_.matmul(bank[k % 2][:, m * 3 * R:(m + 1) * 3 * R], OHT[:, 9 * k + m, :],
                                           W3[:].rearrange("p x r -> p (x r)"), start=(m == 0), stop=True,
                                           skip_group_check=True)
                        mm.then_inc(s["lk"], 1)

                def aggregate(b, par):
                    g_total = pe.value_load(ROWI[0:1, bass.ds(b + (1 + par) * NB, 1)], min_val=16, max_val=16 * G * (NB + 1) // 2)
                    pe.wait_ge(s["ow"], b + 1)
                    pe.wait_ge(gat[par], g_total)
                    if dyn(b) or b >= 2:
                        pe.wait_ge(s["o"], b - 1)
                    for k in range(G):
                        mm = t_.matmul(bank[(2, 5)[par]][:, 0:EMB], OW[:, k, :], Gbuf[par][:, k, :],
                                       start=(k == 0), stop=(k == G - 1))
                    mm.then_inc(s["acc"], 1)

                tables(0, 0, 16)
                tables(1, 1, 16)
                aggregate(0, 0)
                tables(2, 0, 32)
                aggregate(1, 1)
                with pe.Fori(1, (NB - 1) // 2) as j:
                    tables(j * 2 + 1, 1, j * 16 + 16)
                    aggregate(j * 2, 0)
                    tables(j * 2 + 2, 0, j * 16 + 32)
                    aggregate(j * 2 + 1, 1)
                aggregate(NB - 1, 0)
            with pe.If(bad > 0):
                with pe.Fori(0, NCOL) as t:
                    pe.wait_ge(s["g_mask"], t * 4 + 4)
                    pe.wait_ge(s["g_counted"], t * 2 + 2)
                    for k in range(2):
                        mm = t_.matmul(bank[k][:, 0:HALF], gen_node, gen_br_flat[:, k * HALF:(k + 1) * HALF],
                                       start=True, stop=True)
                    mm.then_inc(s["g_cnt_mm"], 1)
                pe.wait_ge(s["g_counted"], NCOL * 2 + 2)
                with pe.Fori(0, NCOL) as t:
                    pe.wait_ge(s["g_mask"], t * 4 + 4 * NCOL + 4)
                    t_.transpose(bank[6][:, 0:EP], gen_node, identf[0:EP, 0:EP]).then_inc(s["g_turn_mm"], 1)
                    pe.wait_ge(s["g_turned"], t + 1)
                    for k in range(2):
                        mm = t_.matmul(bank[k][0:EP, 0:HALF], gen_nodeT, gen_w[:, k * HALF:(k + 1) * HALF],
                                       start=True, stop=True)
                    mm.then_inc(s["g_lk"], 1)
                    pe.wait_ge(s["g_msg"], t + 1)
                    for k in range(GCH):
                        pe.wait_ge(s["g_added"], t * GCH + k + 1)
                        n = min(512, NB * EMB - k * 512)
                        t_.matmul(bank[2 + k % 2][:, 0:n], gen_node, gen_msg_flat[:, k * 512:k * 512 + n],
                                  start=True, stop=True).then_inc(s["g_sum_mm"], 1)

_INS = ["x", "src", "dst", "edge_type_16", "L0_gnn_tokeys", "L0_gnn_toqueries", "L0_gnn_relations",
        "L0_gnn_comps", "L0_gnn_bases_w"]


def kernel(**inputs):
    import numpy as _np
    import concourse.bacc as _bacc
    from concourse import mybir as _mybir
    from concourse.bass_utils import run_bass_kernel_spmd as _run

    nc = _bacc.Bacc("TRN2", target_bir_lowering=False, num_devices=1)
    arrays, args = {}, []
    for name in _INS:
        a = _np.ascontiguousarray(inputs[name])
        arrays[f"in_{name}"] = a
        args.append(nc.dram_tensor(f"in_{name}", a.shape, _mybir.dt.from_np(a.dtype), kind="ExternalInput").ap())
    o = nc.dram_tensor("out_0", inputs["x"].shape, _mybir.dt.float32, kind="ExternalOutput").ap()
    program(nc, *args, o)
    r = _run(nc, [arrays], core_ids=[0])
    return r.results[0]["out_0"]
```
